# Optimizing a Trainium2 kernel written in Bass

```python
import numpy as np
import jax
import jax.numpy as jnp

def _softmax(x, axis=-1):
    return jax.nn.softmax(x, axis=axis)

def _gelu(x):
    return jax.nn.gelu(x, approximate=True)

def _silu(x):
    return jax.nn.silu(x)

def _sigmoid(x):
    return jax.nn.sigmoid(x)

def _layernorm(x, axis=-1, eps=1e-05):
    m = jnp.mean(x, axis=axis, keepdims=True)
    v = jnp.var(x, axis=axis, keepdims=True)
    return (x - m) / jnp.sqrt(v + eps)

def _scatter_add(tgt, idx, src, axis=0):
    return tgt.at[idx].add(src)

def _segment_sum(src, seg, n):
    return jax.ops.segment_sum(src, seg, n)
kernel_name = 'mk_adj_preln_d1_adj_r2_6c73da'

def setup_inputs(seed: int=0):
    np.random.seed(seed)
    _w = jnp.asarray

    def _rec_inputs():
        import jax
        import jax.numpy as jnp
        _gk = jax.random.key(seed)
        x = -0.0005207 + 1.001 * jax.random.normal(jax.random.fold_in(_gk, 1), (16, 512, 128), jnp.float32)
        _a = jax.random.bernoulli(jax.random.fold_in(_gk, 2), 0.03125, (16, 512, 512))
        _a = jnp.logical_or(_a, jnp.swapaxes(_a, -1, -2))
        _a = jnp.logical_or(_a, jnp.eye(512, dtype=bool))
        _af = _a.astype(jnp.float32)
        _af = _af * jax.random.uniform(jax.random.fold_in(_gk, 3), (16, 512, 512), jnp.float32, 0.05, 1)
        adj = _af
        return (x, adj)
    x, adj = _rec_inputs()

    def _L0_gnn_setup():
        import jax, jax.numpy as jnp
        import numpy as np
        B, N, F = (8, 512, 128)
        OUT, REL = (128, 16)
        NADJ = 7
        key = jax.random.key(seed)
        k0, k1, k2, k3, k4 = jax.random.split(key, 5)
        features = jax.random.normal(k0, (B, N, F), dtype=jnp.float32)
        A1 = jax.random.uniform(k1, (B, N, N), dtype=jnp.float32)
        A2 = jax.random.uniform(k2, (B, N, N), dtype=jnp.float32)
        W = jax.random.normal(k3, (NADJ, F + REL, OUT), dtype=jnp.float32) * 0.05
        W_edges = jnp.ones((NADJ, REL), dtype=jnp.float32)
        b = jax.random.uniform(k4, (N, OUT), dtype=jnp.float32, minval=-0.05, maxval=0.05)
        return {'features': features, 'A1': A1, 'A2': A2, 'W': W, 'W_edges': W_edges, 'b': b}
    _L0_gnn_all = _L0_gnn_setup()
    _L0_gnn_in = {k: v for k, v in _L0_gnn_all.items() if k in ('W', 'W_edges', 'b')}
    del _L0_gnn_all
    return {'x': x, 'adj': adj, 'L0_gnn_W': _L0_gnn_in['W'], 'L0_gnn_W_edges': _L0_gnn_in['W_edges'], 'L0_gnn_b': _L0_gnn_in['b']}

def reference(x, adj, L0_gnn_W, L0_gnn_W_edges, L0_gnn_b):
    import jax
    import jax.numpy as jnp

    def _L0_gnn_ref(features, A1, A2, W, W_edges, b):
        import jax, jax.numpy as jnp
        import numpy as np
        B, N, F = (8, 512, 128)
        OUT, REL = (128, 16)
        NADJ = 7
        eye = jnp.zeros_like(A1) + jnp.eye(N, dtype=A1.dtype)
        shifted = jnp.roll(eye, 1, axis=0)
        A_fwd = [A1, A2, shifted]
        A_list = A_fwd + [jnp.swapaxes(a, 1, 2) for a in A_fwd]
        A_list.append(eye)
        A = jnp.stack(A_list, axis=0)
        HW = jnp.einsum('bnf,rfo->rbno', features, W[:, :F]) + jnp.einsum('rd,rdo->ro', W_edges, W[:, F:])[:, None, None, :]
        AHW = jnp.einsum('rbnm,rbmo->rbno', A, HW)
        out = jnp.max(AHW, axis=0) + b
        return out
    h = jnp.maximum(_layernorm(x, axis=-1), 0.0)
    x = x + _L0_gnn_ref(h, adj, adj, L0_gnn_W, L0_gnn_W_edges, L0_gnn_b)
    return x

_drawn_inputs = setup_inputs


def setup_inputs(seed=0):
    import zlib

    import numpy as np

    out = dict(_drawn_inputs(seed))
    spreads = {'L0_gnn_W_edges': (1.0, 0.2)}
    factors = {'L0_gnn_b': 8.0}
    for name, (base, spread) in spreads.items():
        noise = np.random.default_rng([zlib.crc32(name.encode()), seed]).standard_normal(out[name].shape)
        drawn = base * np.exp(spread * noise) if base else spread * noise
        out[name] = jnp.asarray(drawn.astype(out[name].dtype))
    for name, factor in factors.items():
        out[name] = (out[name] * factor).astype(out[name].dtype)
    return out
```

```python
from contextlib import ExitStack

import concourse.bass as bass
from concourse import mybir


def gnn_layer(nc, x, adj, W, W_edges, bias, out):
    fp32 = mybir.dt.float32
    fp32r = mybir.dt.float32r
    ALU = mybir.AluOpType
    ACT = mybir.ActivationFunctionType

    B, N, F = x.shape
    R, FE, O = W.shape
    REL = FE - F
    P = 128
    C = N // P
    EPS = 1e-5
    FWD, BWD, EYE = (0, 1), (3, 4), (2, 5, 6)
    ORDER = (*EYE, *BWD, *FWD)
    BANK = {r: s % 3 for s, r in enumerate(ORDER)}
    BEFORE = {}
    for s, r in enumerate(ORDER):
        earlier = [q for q in ORDER[:s] if BANK[q] == BANK[r]]
        BEFORE[r] = (earlier[-1], 0) if earlier else ([q for q in ORDER if BANK[q] == BANK[r]][-1], 1)
    K4 = 4
    QD = P // C
    RANK1 = (*FWD, *BWD)

    ctx = ExitStack()
    with ctx:
        def sb(name, shape, dt=fp32):
            return ctx.enter_context(nc.sbuf_tensor(name, shape, dt))

        def bank(name):
            return ctx.enter_context(nc.psum_tensor(name, [P, N], fp32))

        def sem(name):
            return ctx.enter_context(nc.semaphore(name))

        def pair(make, name, *args):
            return [make(f"{name}{q}", *args) for q in range(2)]

        ident = sb("ident", [P, P])
        ident_r = sb("ident_r", [P, P], fp32r)
        minus_half, eps, minus_one = (sb(s, [P, C]) for s in ("minus_half", "eps", "minus_one"))
        ones = sb("ones", [P, C, 2])
        w_sb = sb("w_sb", [P, R, O])
        w_hi = sb("w_hi", [P, R, O], fp32r)
        w_lo = sb("w_lo", [P, R, O], fp32r)
        we_sb = sb("we_sb", [REL, R, O])
        wedge = sb("wedge", [REL, R])
        c_col = sb("c_col", [P, R])
        c_parts = sb("c_parts", [P, len(RANK1), C, QD], fp32r)
        c_rows = sb("c_rows", [P, len(RANK1), O], fp32r)
        bias_sb = sb("bias_sb", [P, C, O])

        a_sb = pair(sb, "a_sb", [P, C, N])
        a_hi = pair(sb, "a_hi", [P, C, N], fp32r)
        a_lo = pair(sb, "a_lo", [P, C, N], fp32r)
        at_hi = pair(sb, "at_hi", [P, C, N], fp32r)
        at_lo = pair(sb, "at_lo", [P, C, N], fp32r)
        x_sb = pair(sb, "x_sb", [P, C, F])
        xb_sb = pair(sb, "xb_sb", [P, C, F])
        h_sb = pair(sb, "h_sb", [P, C, F])
        h_hi = pair(sb, "h_hi", [P, C, F], fp32r)
        h_lo = pair(sb, "h_lo", [P, C, F], fp32r)
        ht_hi = pair(sb, "ht_hi", [P, N], fp32r)
        ht_lo = pair(sb, "ht_lo", [P, N], fp32r)
        stats = pair(sb, "stats", [P, C, 6])
        mean_var = pair(sb, "mean_var", [P, C, 2])
        var_eps = pair(sb, "var_eps", [P, C])
        neg_mean = pair(sb, "neg_mean", [P, C])
        rstd = pair(sb, "rstd", [P, C])
        shift = pair(sb, "shift", [P, C])
        sums = pair(sb, "sums", [P, 2, C])
        sum_parts = pair(sb, "sum_parts", [P, C, QD], fp32r)
        fwd_hi = sb("fwd_hi", [P, N], fp32r)
        fwd_lo = sb("fwd_lo", [P, N], fp32r)
        bwd_hi = sb("bwd_hi", [P, N], fp32r)
        bwd_lo = sb("bwd_lo", [P, N], fp32r)
        sum_rows = sb("sum_rows", [P, N], fp32r)
        best = sb("best", [P, N])
        o_sb = pair(sb, "o_sb", [P, C, O])

        at_ps = pair(bank, "at_ps")
        misc_ps = bank("misc_ps")
        fwd_ps = bank("fwd_ps")
        bwd_ps = bank("bwd_ps")
        rel_ps = [bank(f"rel_ps{q}") for q in range(3)]

        def at_bank(b, i):
            return rel_ps[i - 1] if isinstance(b, int) and b == 0 and i >= 2 else at_ps[i % 2]

        w_loaded, we_loaded, wedge_loaded, bias_loaded = (
            sem(s) for s in ("w_loaded", "we_loaded", "wedge_loaded", "bias_loaded"))
        a_loaded = [[sem(f"a_loaded{q}_{j}") for j in range(C)] for q in range(2)]
        x_loaded = pair(sem, "x_loaded")
        out_stored = pair(sem, "out_stored")
        ident_zeroed, ident_ready, consts_ready = sem("ident_zeroed"), sem("ident_ready"), sem("consts_ready")
        ident_r_ready, parts_zeroed = sem("ident_r_ready"), sem("parts_zeroed")
        c_multiplied, c_ready, c_zeroed, c_hi_ready, c_split = (
            sem(s) for s in ("c_multiplied", "c_ready", "c_zeroed", "c_hi_ready", "c_split"))
        c_turned, c_rows_ready = sem("c_turned"), sem("c_rows_ready")
        w_hi_ready, w_lo_ready = sem("w_hi_ready"), sem("w_lo_ready")
        bn_done, mean_var_ready, ve_ready, rstd_ready, shift_ready = (
            sem(s) for s in ("bn_done", "mean_var_ready", "ve_ready", "rstd_ready", "shift_ready"))
        h_ready, h_hi_ready, h_lo_ready = sem("h_ready"), sem("h_hi_ready"), sem("h_lo_ready")
        h_turned, ht_hi_ready, ht_lo_ready = sem("h_turned"), sem("ht_hi_ready"), sem("ht_lo_ready")
        a_hi_ready = [sem(f"a_hi_ready{j}") for j in range(C)]
        a_lo_ready = [sem(f"a_lo_ready{j}") for j in range(C)]
        a_turned = [sem(f"a_turned{i}") for i in range(C)]
        at_hi_ready = [sem(f"at_hi_ready{i}") for i in range(C)]
        at_lo_ready = [sem(f"at_lo_ready{i}") for i in range(C)]
        sum_hi_ready, sums_split = sem("sum_hi_ready"), sem("sums_split")
        sums_turned, sum_rows_ready = sem("sums_turned"), sem("sum_rows_ready")
        xb_ready = sem("xb_ready")
        fwd_done, fwd_hi_ready, fwd_lo_ready = sem("fwd_done"), sem("fwd_hi_ready"), sem("fwd_lo_ready")
        bwd_done, bwd_hi_ready, bwd_lo_ready = sem("bwd_done"), sem("bwd_hi_ready"), sem("bwd_lo_ready")
        rel_done = [sem(f"rel_done{r}") for r in range(R)]
        joined = [sem(f"joined{r}") for r in range(R)]
        best_turned, out_ready = sem("best_turned"), sem("out_ready")

        def wait(eng, semaphore, count):
            if not isinstance(count, int) or count > 0:
                eng.wait_ge(semaphore, count)

        def after(k, q):
            return (k, 1) if q == 0 else (k + 1, 0)

        def before(k, q):
            return (k, 0) if q == 1 else (k - 1, 1)

        PAIRS = B // 2

        def all_batches(eng, step):
            step(0, 0, True, 2)
            step(0, 1, False, 2)
            with eng.Fori(1, PAIRS - 1) as k:
                step(k, 0, False, 2)
                step(k, 1, False, 2)
            step(PAIRS - 1, 0, False, 1)
            step(PAIRS - 1, 1, False, 0)

        block = ctx.enter_context(nc.Block())

        @block.sync
        def _(sp):
            def load_x(k, q):
                sp.dma_start(x_sb[q][:], x[2 * k + q, :, :].rearrange("(j p) f -> p j f", p=P)).then_inc(x_loaded[q], 16)

            def load_a(k, q, j):
                sp.dma_start(a_sb[q][:, j, :], adj[2 * k + q, j * P:(j + 1) * P, :]).then_inc(a_loaded[q][j], 16)

            def reload(k, q):
                b = 2 * k + q
                sp.wait_ge(h_ready, b + 1)
                sp.wait_ge(xb_ready, b + 1)
                load_x(k + 1, q)
                sp.wait_ge(a_turned[C - 1], b + 1)
                for j in range(C):
                    sp.wait_ge(a_lo_ready[j], b + 1)
                    load_a(k + 1, q, j)

            def store(k, q):
                sp.wait_ge(out_ready, 2 * k + q + 1)
                sp.dma_start(out[2 * k + q, :, :].rearrange("(j p) o -> p j o", p=P), o_sb[q][:]).then_inc(out_stored[q], 16)

            load_x(0, 0)
            for j in range(C):
                load_a(0, 0, j)
            load_x(0, 1)
            for j in range(C):
                load_a(0, 1, j)
            reload(0, 0)
            reload(0, 1)
            with sp.Fori(0, PAIRS - 2) as k:
                store(k, 0)
                reload(k + 1, 0)
                store(k, 1)
                reload(k + 1, 1)
            for k in (PAIRS - 2, PAIRS - 1):
                store(k, 0)
                store(k, 1)
            sp.wait_ge(out_stored[0], 16 * PAIRS)
            sp.wait_ge(out_stored[1], 16 * PAIRS)

        @block.gpsimd
        def _(pool):
            def reciprocal_std(k, q):
                b = 2 * k + q
                pool.wait_ge(mean_var_ready, b + 1)
                wait(pool, h_ready, b - 1)
                pool.tensor_tensor(var_eps[q][:], mean_var[q][:, :, 1], eps[:], ALU.add)
                pool.tensor_tensor(neg_mean[q][:], mean_var[q][:, :, 0], minus_one[:], ALU.mult).then_inc(ve_ready, 1)
                pool.wait_ge(ve_ready, b + 1)
                pool.tensor_tensor(rstd[q][:], var_eps[q][:], minus_half[:], ALU.pow).then_inc(rstd_ready, 1)
                pool.wait_ge(rstd_ready, b + 1)
                pool.tensor_tensor(shift[q][:], neg_mean[q][:], rstd[q][:], ALU.mult).then_inc(shift_ready, 1)

            def split_a(k, q, j):
                b = 2 * k + q
                pool.wait_ge(a_hi_ready[j], b + 1)
                wait(pool, bwd_done, b - 1)
                pool.tensor_tensor(a_lo[q][:, j, :], a_sb[q][:, j, :], a_hi[q][:, j, :].bitcast(fp32),
                                   ALU.subtract).then_inc(a_lo_ready[j], 1)

            def split_h(k, q):
                b = 2 * k + q
                pool.wait_ge(h_hi_ready, b + 1)
                wait(pool, fwd_done, b - 1)
                pool.tensor_tensor(h_lo[q][:], h_sb[q][:], h_hi[q][:].bitcast(fp32),
                                   ALU.subtract).then_inc(h_lo_ready, 1)

            def add_bias(k, q):
                b = 2 * k + q
                pool.wait_ge(x_loaded[q], 16 * (k + 1))
                wait(pool, out_ready, b - 1)
                pool.tensor_tensor(xb_sb[q][:], x_sb[q][:], bias_sb[:], ALU.add).then_inc(xb_ready, 1)

            def split_sums(k, q):
                b = 2 * k + q
                wait(pool, sums_turned, b - 1)
                pool.wait_ge(a_hi_ready[C - 1], b + 1)
                pool.wait_ge(at_hi_ready[C - 1], b + 1)
                for t in range(2):
                    both = sums[q][:, t, :].unsqueeze(2).to_broadcast([P, C, 2])
                    last = pool.tensor_tensor(sum_parts[q][:, :, K4 * t:K4 * t + K4:2], both, ones[:], ALU.mult)
                last.then_inc(sum_hi_ready, 1)
                pool.wait_ge(sum_hi_ready, b + 1)
                for t in range(2):
                    both = sums[q][:, t, :].unsqueeze(2).to_broadcast([P, C, 2])
                    last = pool.tensor_tensor(sum_parts[q][:, :, K4 * t + 1:K4 * t + K4:2], both,
                                              sum_parts[q][:, :, K4 * t:K4 * t + K4:2].bitcast(fp32), ALU.subtract)
                last.then_inc(sums_split, 1)

            def step(k, q, first, left):
                split_sums(k, q)
                if left:
                    ahead = after(k, q)
                    reciprocal_std(*ahead)
                    split_a(*ahead, 0)
                    split_a(*ahead, 1)
                    split_a(*ahead, 2)
                    split_h(*ahead)
                    split_a(*ahead, 3)
                    add_bias(*ahead)

            pool.dma_start(we_sb[:], W[:, F:FE, :].rearrange("r d o -> d r o")).then_inc(we_loaded, 16)
            with nc.allow_non_contiguous_dma(reason="a few hundred bytes, once"):
                pool.dma_start(wedge[:], W_edges.rearrange("r d -> d r")).then_inc(wedge_loaded, 16)
            pool.dma_start(w_sb[:], W[:, 0:F, :].rearrange("r f o -> f r o")).then_inc(w_loaded, 16)
            pool.dma_start(bias_sb[:], bias.rearrange("(j p) o -> p j o", p=P)).then_inc(bias_loaded, 16)
            pool.memset(ident[:], 0.0).then_inc(ident_zeroed, 1)
            pool.memset(minus_half[:], -0.5)
            pool.memset(eps[:], EPS)
            pool.memset(minus_one[:], -1.0)
            pool.memset(ones[:], 1.0).then_inc(consts_ready, 1)
            pool.wait_ge(ident_zeroed, 1)
            pool.affine_select(out=ident[:], in_=ident[:], compare_op=ALU.not_equal, fill=1.0, base=0,
                               pattern=[[-1, P]], channel_multiplier=1).then_inc(ident_ready, 1)
            pool.wait_ge(consts_ready, 1)
            for q in range(2):
                pool.memset(sum_parts[q][:].bitcast(fp32), 0.0)
            pool.memset(sum_rows[:].bitcast(fp32), 0.0).then_inc(parts_zeroed, 1)
            reciprocal_std(0, 0)
            pool.wait_ge(w_hi_ready, 1)
            pool.tensor_tensor(w_lo[:], w_sb[:], w_hi[:].bitcast(fp32), ALU.subtract).then_inc(w_lo_ready, 1)
            pool.wait_ge(bias_loaded, 16)
            add_bias(0, 0)
            pool.wait_ge(parts_zeroed, 1)
            all_batches(pool, step)

        @block.scalar
        def _(act):
            def round_a(k, q, j):
                b = 2 * k + q
                act.wait_ge(a_loaded[q][j], 16 * (k + 1))
                wait(act, bwd_done, b - 1)
                wait(act, sums_split, b - 1)
                act.activation(a_hi[q][:, j, :], a_sb[q][:, j, :], ACT.Copy,
                               accum_out=sums[q][:, 0, j:j + 1]).then_inc(a_hi_ready[j], 1)

            def round_at(k, q, i):
                b = 2 * k + q
                act.wait_ge(a_turned[i], b + 1)
                wait(act, fwd_done, b - 1)
                act.activation(at_hi[q][:, i, :], at_bank(b, i)[:], ACT.Copy,
                               accum_out=sums[q][:, 1, i:i + 1]).then_inc(at_hi_ready[i], 1)

            def normalise(k, q):
                b = 2 * k + q
                act.wait_ge(x_loaded[q], 16 * (k + 1))
                act.wait_ge(shift_ready, b + 1)
                wait(act, h_lo_ready, b - 1)
                wait(act, h_turned, b - 1)
                for j in range(C):
                    last = act.activation(h_sb[q][:, j, :], x_sb[q][:, j, :], ACT.Relu,
                                          bias=shift[q][:, j:j + 1], scale=rstd[q][:, j:j + 1])
                last.then_inc(h_ready, 1)

            def round_ht(k, q):
                b = 2 * k + q
                act.wait_ge(h_turned, b + 1)
                wait(act, rel_done[EYE[-1]], b - 1)
                act.activation(ht_hi[q][:], misc_ps[:], ACT.Copy).then_inc(ht_hi_ready, 1)

            def round_fwd(b):
                act.wait_ge(fwd_done, b + 1)
                wait(act, rel_done[FWD[-1]], b)
                act.activation(fwd_hi[:], fwd_ps[:], ACT.Copy).then_inc(fwd_hi_ready, 1)

            def round_bwd(b):
                act.wait_ge(bwd_done, b + 1)
                wait(act, rel_done[BWD[-1]], b)
                act.activation(bwd_hi[:], bwd_ps[:], ACT.Copy).then_inc(bwd_hi_ready, 1)

            def rows_of_sums(b):
                act.wait_ge(sums_turned, b + 1)
                wait(act, rel_done[FWD[-1]], b)
                for j in range(C):
                    rows = slice(j * QD, (j + 1) * QD)
                    last = act.activation(sum_rows[rows, j * P:(j + 1) * P], misc_ps[rows, 0:P], ACT.Copy)
                last.then_inc(sum_rows_ready, 1)

            def join_first(b):
                r = ORDER[0]
                act.wait_ge(rel_done[r], b + 1)
                wait(act, best_turned, b)
                act.activation(best[:], rel_ps[BANK[r]][:], ACT.Identity,
                               bias=c_col[:, r:r + 1]).then_inc(joined[r], 1)

            def step(k, q, first, left):
                b = 2 * k + q
                if left:
                    ahead = after(k, q)
                    round_a(*ahead, 0)
                    round_a(*ahead, 1)
                    round_at(*ahead, 0)
                    round_a(*ahead, 2)
                    round_at(*ahead, 1)
                round_bwd(b)
                if left:
                    normalise(*ahead)
                    round_at(*ahead, 2)
                rows_of_sums(b)
                if left:
                    round_a(*ahead, 3)
                round_fwd(b)
                join_first(b)
                if left:
                    round_at(*ahead, 3)
                    round_ht(*ahead)

            act.wait_ge(ident_ready, 1)
            act.activation(ident_r[:], ident[:], ACT.Copy).then_inc(ident_r_ready, 1)
            for j in range(C):
                round_a(0, 0, j)
            normalise(0, 0)
            for i in range(C):
                round_at(0, 0, i)
            round_ht(0, 0)
            act.wait_ge(w_loaded, 16)
            act.activation(w_hi[:], w_sb[:], ACT.Copy).then_inc(w_hi_ready, 1)
            act.wait_ge(c_turned, 1)
            act.activation(c_rows[:].rearrange("k r o -> k (r o)"), rel_ps[0][:], ACT.Copy).then_inc(c_rows_ready, 1)
            act.wait_ge(c_ready, 1)
            act.wait_ge(parts_zeroed, 1)
            all_batches(act, step)

        @block.vector
        def _(dve):
            def moments(k, q):
                b = 2 * k + q
                dve.wait_ge(x_loaded[q], 16 * (k + 1))
                for j in range(C):
                    last = dve.bn_stats(stats[q][:, j, :], x_sb[q][:, j, :])
                last.then_inc(bn_done, 1)

            def mean_and_variance(k, q):
                for j in range(C):
                    last = dve.bn_aggr(mean_var[q][:, j, :], stats[q][:, j, :])
                last.then_inc(mean_var_ready, 1)

            def round_h(k, q):
                b = 2 * k + q
                dve.wait_ge(h_ready, b + 1)
                wait(dve, fwd_done, b - 1)
                dve.tensor_copy(h_hi[q][:], h_sb[q][:]).then_inc(h_hi_ready, 1)

            def split_at(k, q, i):
                b = 2 * k + q
                dve.wait_ge(at_hi_ready[i], b + 1)
                wait(dve, fwd_done, b - 1)
                dve.tensor_tensor(at_lo[q][:, i, :], at_bank(b, i)[:], at_hi[q][:, i, :].bitcast(fp32),
                                  ALU.subtract).then_inc(at_lo_ready[i], 1)

            def split_ht(k, q):
                b = 2 * k + q
                dve.wait_ge(ht_hi_ready, b + 1)
                wait(dve, rel_done[EYE[-1]], b - 1)
                dve.tensor_tensor(ht_lo[q][:], misc_ps[:], ht_hi[q][:].bitcast(fp32),
                                  ALU.subtract).then_inc(ht_lo_ready, 1)

            def split_fwd(b):
                dve.wait_ge(fwd_hi_ready, b + 1)
                dve.tensor_tensor(fwd_lo[:], fwd_ps[:], fwd_hi[:].bitcast(fp32),
                                  ALU.subtract).then_inc(fwd_lo_ready, 1)

            def split_bwd(b):
                dve.wait_ge(bwd_hi_ready, b + 1)
                dve.tensor_tensor(bwd_lo[:], bwd_ps[:], bwd_hi[:].bitcast(fp32),
                                  ALU.subtract).then_inc(bwd_lo_ready, 1)

            def join(b, s):
                r = ORDER[s]
                dve.wait_ge(rel_done[r], b + 1)
                dve.wait_ge(joined[ORDER[s - 1]], b + 1)
                if r in EYE:
                    dve.scalar_tensor_tensor(out=best[:], in0=rel_ps[BANK[r]][:], scalar=c_col[:, r:r + 1],
                                             in1=best[:], op0=ALU.add, op1=ALU.max).then_inc(joined[r], 1)
                else:
                    dve.tensor_tensor(best[:], rel_ps[BANK[r]][:], best[:], ALU.max).then_inc(joined[r], 1)

            def finish(k, q):
                b = 2 * k + q
                dve.wait_ge(best_turned, b + 1)
                dve.wait_ge(xb_ready, b + 1)
                wait(dve, out_stored[q], 16 * k)
                dve.tensor_tensor(o_sb[q][:].rearrange("p j o -> p (j o)"), misc_ps[:],
                                  xb_sb[q][:].rearrange("p j o -> p (j o)"), ALU.add).then_inc(out_ready, 1)

            def step(k, q, first, left):
                b = 2 * k + q
                if left:
                    ahead = after(k, q)
                    split_at(*ahead, 0)
                    split_at(*ahead, 1)
                if not first:
                    finish(*before(k, q))
                split_bwd(b)
                if left:
                    round_h(*ahead)
                    split_at(*ahead, 2)
                if left > 1:
                    moments(k + 1, q)
                    dve.wait_ge(bn_done, b + 3)
                split_fwd(b)
                if left > 1:
                    mean_and_variance(k + 1, q)
                join(b, 1)
                if left:
                    split_at(*ahead, 3)
                join(b, 2)
                join(b, 3)
                join(b, 4)
                if left:
                    split_ht(*ahead)
                join(b, 5)
                join(b, 6)

            dve.memset(c_parts[:].bitcast(fp32), 0.0).then_inc(c_zeroed, 1)
            moments(0, 0)
            dve.wait_ge(bn_done, 1)
            mean_and_variance(0, 0)
            for j in range(C):
                dve.wait_ge(a_hi_ready[j], 1)
                dve.tensor_tensor(a_lo[0][:, j, :], a_sb[0][:, j, :], a_hi[0][:, j, :].bitcast(fp32),
                                  ALU.subtract).then_inc(a_lo_ready[j], 1)
            dve.wait_ge(c_multiplied, 1)
            dve.tensor_copy(c_col[:], rel_ps[0][:, 0:R]).then_inc(c_ready, 1)
            dve.wait_ge(c_ready, 1)
            dve.wait_ge(c_zeroed, 1)

            def c_part(r, part):
                s, at = RANK1.index(r), K4 * (r in BWD) + 2 * part
                return c_parts[:, s, :, at:at + 2], c_col[:, r:r + 1].unsqueeze(2).to_broadcast([P, C, 2])

            for r in RANK1:
                hi, c = c_part(r, 0)
                last = dve.tensor_copy(hi, c)
            last.then_inc(c_hi_ready, 1)
            dve.wait_ge(c_hi_ready, 1)
            for r in RANK1:
                (hi, c), (lo, _) = c_part(r, 0), c_part(r, 1)
                last = dve.tensor_tensor(lo, c, hi.bitcast(fp32), ALU.subtract)
            last.then_inc(c_split, 1)
            round_h(0, 0)
            dve.wait_ge(h_hi_ready, 1)
            dve.tensor_tensor(h_lo[0][:], h_sb[0][:], h_hi[0][:].bitcast(fp32), ALU.subtract).then_inc(h_lo_ready, 1)
            for i in range(C):
                split_at(0, 0, i)
            split_ht(0, 0)
            moments(0, 1)
            dve.wait_ge(bn_done, 2)
            mean_and_variance(0, 1)
            all_batches(dve, step)
            finish(PAIRS - 1, 1)

        @block.tensor
        def _(pe):
            def turn_a(k, q, i):
                b = 2 * k + q
                if i == 0:
                    for j in range(C):
                        pe.wait_ge(a_loaded[q][j], 16 * (k + 1))
                if not (isinstance(b, int) and b == 0):
                    before_it = b + 1 if i >= 2 else 1 if isinstance(b, int) and b == 1 else b
                    pe.wait_ge(at_lo_ready[i % 2 if i >= 2 or before_it is 1 else i + 2], before_it)
                for j in range(C):
                    last = pe.transpose(at_bank(b, i)[:, j * P:(j + 1) * P], a_sb[q][:, j, i * P:(i + 1) * P], ident[:])
                last.then_inc(a_turned[i], 1)

            def turn_h(k, q):
                b = 2 * k + q
                pe.wait_ge(h_ready, b + 1)
                wait(pe, sum_rows_ready, b)
                for j in range(C):
                    last = pe.transpose(misc_ps[:, j * P:(j + 1) * P], h_sb[q][:, j, :], ident[:])
                last.then_inc(h_turned, 1)

            def turn_sums(k, q, first):
                b = 2 * k + q
                pe.wait_ge(sums_split, b + 1)
                if first:
                    pe.wait_ge(ht_lo_ready, 1)
                else:
                    pe.wait_ge(out_ready, b)
                pe.matmul(misc_ps[:, 0:P], sum_parts[q][:].rearrange("p j k -> p (j k)"), ident_r[:],
                          start=True, stop=True).then_inc(sums_turned, 1)

            def turn_best(k, q, last_batch=False):
                b = 2 * k + q
                pe.wait_ge(joined[ORDER[-1]], b + 1)
                if last_batch:
                    pe.wait_ge(sum_rows_ready, b + 1)
                else:
                    pe.wait_ge(ht_lo_ready, b + 2)
                for j in range(C):
                    last = pe.transpose(misc_ps[:, j * P:(j + 1) * P], best[:, j * P:(j + 1) * P], ident[:])
                last.then_inc(best_turned, 1)

            def passes(out, w_hi_, w_lo_, m_hi, m_lo, start, stop):
                pe.matmul(out, w_hi_, m_hi, start=start, stop=False)
                pe.matmul(out, w_hi_, m_lo, start=False, stop=False)
                return pe.matmul(out, w_lo_, m_hi, start=False, stop=stop)

            def bwd(k, q, j):
                b = 2 * k + q
                if j == 0:
                    pe.wait_ge(h_hi_ready, b + 1)
                    pe.wait_ge(h_lo_ready, b + 1)
                    wait(pe, bwd_lo_ready, b)
                pe.wait_ge(a_hi_ready[j], b + 1)
                pe.wait_ge(a_lo_ready[j], b + 1)
                last = passes(bwd_ps[:], h_hi[q][:, j, :], h_lo[q][:, j, :], a_hi[q][:, j, :], a_lo[q][:, j, :],
                              j == 0, j == C - 1)
                if j == C - 1:
                    last.then_inc(bwd_done, 1)

            def fwd(k, q, i):
                b = 2 * k + q
                if i == 0:
                    wait(pe, fwd_lo_ready, b)
                pe.wait_ge(at_hi_ready[i], b + 1)
                pe.wait_ge(at_lo_ready[i], b + 1)
                last = passes(fwd_ps[:], h_hi[q][:, i, :], h_lo[q][:, i, :], at_hi[q][:, i, :], at_lo[q][:, i, :],
                              i == 0, i == C - 1)
                if i == C - 1:
                    last.then_inc(fwd_done, 1)

            def relation(k, q, r):
                b = 2 * k + q
                prior, back = BEFORE[r]
                wait(pe, joined[prior], b + 1 - back)
                if r == EYE[0]:
                    pe.wait_ge(ht_hi_ready, b + 1)
                    pe.wait_ge(ht_lo_ready, b + 1)
                elif r == BWD[0]:
                    pe.wait_ge(bwd_hi_ready, b + 1)
                    pe.wait_ge(bwd_lo_ready, b + 1)
                    pe.wait_ge(sum_rows_ready, b + 1)
                elif r == FWD[0]:
                    pe.wait_ge(fwd_hi_ready, b + 1)
                    pe.wait_ge(fwd_lo_ready, b + 1)
                m_hi, m_lo = ((ht_hi[q], ht_lo[q]) if r in EYE else (bwd_hi, bwd_lo) if r in BWD else (fwd_hi, fwd_lo))
                to = rel_ps[BANK[r]][:]
                last = passes(to, w_hi[:, r, :], w_lo[:, r, :], m_hi[:], m_lo[:], True, r in EYE)
                if r not in EYE:
                    last = pe.matmul(to, c_rows[:, RANK1.index(r), :], sum_rows[:], start=False, stop=True)
                last.then_inc(rel_done[r], 1)

            def step(k, q, first, left):
                ahead = after(k, q)
                bwd(k, q, 0)
                if left:
                    turn_a(*ahead, 0)
                bwd(k, q, 1)
                bwd(k, q, 2)
                if left:
                    turn_a(*ahead, 1)
                bwd(k, q, 3)
                if not first:
                    turn_best(*before(k, q))
                fwd(k, q, 0)
                fwd(k, q, 1)
                if left:
                    turn_a(*ahead, 2)
                turn_sums(k, q, first)
                fwd(k, q, 2)
                fwd(k, q, 3)
                if first:
                    pe.wait_ge(w_hi_ready, 1)
                    pe.wait_ge(w_lo_ready, 1)
                    pe.wait_ge(c_rows_ready, 1)
                relation(k, q, EYE[0])
                if left:
                    turn_a(*ahead, 3)
                relation(k, q, EYE[1])
                relation(k, q, EYE[2])
                relation(k, q, BWD[0])
                relation(k, q, BWD[1])
                if left:
                    turn_h(*ahead)
                relation(k, q, FWD[0])
                relation(k, q, FWD[1])

            pe.wait_ge(we_loaded, 16)
            pe.wait_ge(wedge_loaded, 16)
            for r in range(R):
                last = pe.matmul(rel_ps[0][:, r:r + 1], we_sb[:, r, :], wedge[:, r:r + 1], start=True, stop=True)
            last.then_inc(c_multiplied, 1)
            pe.wait_ge(ident_ready, 1)
            for i in range(C):
                turn_a(0, 0, i)
            turn_h(0, 0)
            pe.wait_ge(c_split, 1)
            pe.wait_ge(ident_r_ready, 1)
            for s in range(len(RANK1)):
                last = pe.matmul(rel_ps[0][:, s * O:(s + 1) * O], c_parts[:, s, :, :].rearrange("p j k -> p (j k)"),
                                 ident_r[:], start=True, stop=True)
            last.then_inc(c_turned, 1)
            all_batches(pe, step)
            turn_best(PAIRS - 1, 1, last_batch=True)


_INS = ["x", "adj", "L0_gnn_W", "L0_gnn_W_edges", "L0_gnn_b"]


def kernel(**inputs):
    import numpy as np
    import concourse.bacc as bacc
    from concourse import mybir
    from concourse.bass_utils import run_bass_kernel_spmd

    nc = bacc.Bacc("TRN2", target_bir_lowering=False, num_devices=1)
    arrays, args = {}, []
    for name in _INS:
        a = np.ascontiguousarray(inputs[name])
        arrays[f"in_{name}"] = a
        args.append(nc.dram_tensor(f"in_{name}", a.shape, mybir.dt.from_np(a.dtype), kind="ExternalInput").ap())
    out = nc.dram_tensor("out", inputs["x"].shape, mybir.dt.float32, kind="ExternalOutput").ap()
    gnn_layer(nc, *args, out)
    r = run_bass_kernel_spmd(nc, [arrays], core_ids=[0])
    return r.results[0]["out"]
```

```python
from contextlib import ExitStack

import concourse.bass as bass
from concourse import mybir


def gnn_layer(nc, x, adj, W, W_edges, bias, out):
    fp32 = mybir.dt.float32
    fp32r = mybir.dt.float32r
    ALU = mybir.AluOpType
    ACT = mybir.ActivationFunctionType

    B, N, F = x.shape
    R, FE, O = W.shape
    REL = FE - F
    P = 128
    C = N // P
    EPS = 1e-5
    W_DVE = R // 2
    WARM = 8
    FWD, BWD, EYE = (0, 1), (3, 4), (2, 5, 6)
    ORDER = (*EYE, *BWD, *FWD)
    BANK = {r: s % 3 for s, r in enumerate(ORDER)}
    BEFORE = {}
    for s, r in enumerate(ORDER):
        earlier = [q for q in ORDER[:s] if BANK[q] == BANK[r]]
        BEFORE[r] = (earlier[-1], 0) if earlier else ([q for q in ORDER if BANK[q] == BANK[r]][-1], 1)
    RANK1 = (*FWD, *BWD)
    G = len(RANK1)
    QUARTER = P // G
    K4 = 4

    ctx = ExitStack()
    with ctx:
        def sb(name, shape, dt=fp32):
            return ctx.enter_context(nc.sbuf_tensor(name, shape, dt))

        def bank(name):
            return ctx.enter_context(nc.psum_tensor(name, [P, N], fp32))

        def sem(name):
            return ctx.enter_context(nc.semaphore(name))

        def pair(make, name, *args):
            return [make(f"{name}{q}", *args) for q in range(2)]

        ident = sb("ident", [P, P])
        ident_r = sb("ident_r", [P, P], fp32r)
        minus_half, eps, minus_one = (sb(s, [P, C]) for s in ("minus_half", "eps", "minus_one"))
        ones = sb("ones", [P, 2, C, 2])
        w_sb = sb("w_sb", [P, R, O])
        w_hi = sb("w_hi", [P, R, O], fp32r)
        w_lo = sb("w_lo", [P, R, O], fp32r)
        we_sb = sb("we_sb", [R * REL, O])
        wedge = sb("wedge", [R * REL, 1])
        own_relation = sb("own_relation", [R * REL, R])
        wedge_cols = sb("wedge_cols", [R * REL, R])
        c_col = sb("c_col", [P, R])
        own_chunk = sb("own_chunk", [P, QUARTER // K4])
        c_parts = sb("c_parts", [P, G, QUARTER], fp32r)
        c_rows = sb("c_rows", [P, O], fp32r)
        bias_sb = sb("bias_sb", [P, C, O])
        warm = sb("warm", [P, N], fp32r)

        a_sb = pair(sb, "a_sb", [P, C, N])
        a_hi = pair(sb, "a_hi", [P, C, N], fp32r)
        a_lo = pair(sb, "a_lo", [P, C, N], fp32r)
        at_hi = pair(sb, "at_hi", [P, C, N], fp32r)
        at_lo = pair(sb, "at_lo", [P, C, N], fp32r)
        x_sb = pair(sb, "x_sb", [P, C, F])
        xb_sb = pair(sb, "xb_sb", [P, C, F])
        h_sb = pair(sb, "h_sb", [P, C, F])
        h_hi = pair(sb, "h_hi", [P, C, F], fp32r)
        h_lo = pair(sb, "h_lo", [P, C, F], fp32r)
        ht_hi = pair(sb, "ht_hi", [P, N], fp32r)
        ht_lo = pair(sb, "ht_lo", [P, N], fp32r)
        stats = pair(sb, "stats", [P, C, 6])
        mean_var = pair(sb, "mean_var", [P, C, 2])
        var_eps = pair(sb, "var_eps", [P, C])
        neg_mean = pair(sb, "neg_mean", [P, C])
        rstd = pair(sb, "rstd", [P, C])
        shift = pair(sb, "shift", [P, C])
        sums = pair(sb, "sums", [P, 2, C])
        sum_parts = pair(sb, "sum_parts", [P, G, QUARTER], fp32r)
        fwd_hi = sb("fwd_hi", [P, N], fp32r)
        fwd_lo = sb("fwd_lo", [P, N], fp32r)
        bwd_hi = sb("bwd_hi", [P, N], fp32r)
        bwd_lo = sb("bwd_lo", [P, N], fp32r)
        sum_rows = sb("sum_rows", [P, N], fp32r)
        best = sb("best", [P, N])
        o_sb = pair(sb, "o_sb", [P, C, O])

        at_ps = pair(bank, "at_ps")
        misc_ps = bank("misc_ps")
        fwd_ps = bank("fwd_ps")
        bwd_ps = bank("bwd_ps")
        rel_ps = [bank(f"rel_ps{q}") for q in range(3)]

        def at_bank(b, i):
            return rel_ps[i] if isinstance(b, int) and b == 0 and i < 3 else at_ps[i % 2]

        w_loaded, we_loaded, wedge_loaded, bias_loaded = (
            sem(s) for s in ("w_loaded", "we_loaded", "wedge_loaded", "bias_loaded"))
        a_loaded = [[sem(f"a_loaded{q}_{j}") for j in range(C)] for q in range(2)]
        x_loaded = pair(sem, "x_loaded")
        out_stored = pair(sem, "out_stored")
        ident_zeroed, ident_ready, consts_ready = sem("ident_zeroed"), sem("ident_ready"), sem("consts_ready")
        ident_r_ready, parts_zeroed = sem("ident_r_ready"), sem("parts_zeroed")
        warm_zeroed, own_chunk_ready = sem("warm_zeroed"), sem("own_chunk_ready")
        own_relation_ready, wedge_cols_ready = sem("own_relation_ready"), sem("wedge_cols_ready")
        h0_ready, h0_hi_ready, h0_lo_ready = sem("h0_ready"), sem("h0_hi_ready"), sem("h0_lo_ready")
        c_multiplied, c_ready, c_zeroed, c_hi_ready, c_split = (
            sem(s) for s in ("c_multiplied", "c_ready", "c_zeroed", "c_hi_ready", "c_split"))
        c_turned, c_rows_ready = sem("c_turned"), sem("c_rows_ready")
        w_hi_ready, w_lo_ready = sem("w_hi_ready"), sem("w_lo_ready")
        bn_done, mean_var_ready, ve_ready, rstd_ready, shift_ready = (
            sem(s) for s in ("bn_done", "mean_var_ready", "ve_ready", "rstd_ready", "shift_ready"))
        h_ready, h_hi_ready, h_lo_ready = sem("h_ready"), sem("h_hi_ready"), sem("h_lo_ready")
        h_turned, ht_hi_ready, ht_lo_ready = sem("h_turned"), sem("ht_hi_ready"), sem("ht_lo_ready")
        a_hi_ready = [sem(f"a_hi_ready{j}") for j in range(C)]
        a_lo_ready = [sem(f"a_lo_ready{j}") for j in range(C)]
        a_turned = [sem(f"a_turned{i}") for i in range(C)]
        at_hi_ready = [sem(f"at_hi_ready{i}") for i in range(C)]
        at_lo_ready = [sem(f"at_lo_ready{i}") for i in range(C)]
        sum_hi_ready, sums_split = sem("sum_hi_ready"), sem("sums_split")
        sums_turned, sum_rows_ready = sem("sums_turned"), sem("sum_rows_ready")
        xb_ready = sem("xb_ready")
        fwd_done, fwd_hi_ready, fwd_lo_ready = sem("fwd_done"), sem("fwd_hi_ready"), sem("fwd_lo_ready")
        bwd_done, bwd_hi_ready, bwd_lo_ready = sem("bwd_done"), sem("bwd_hi_ready"), sem("bwd_lo_ready")
        rel_done = [sem(f"rel_done{r}") for r in range(R)]
        joined = [sem(f"joined{r}") for r in range(R)]
        best_turned, out_ready = sem("best_turned"), sem("out_ready")
        half_done, half_joined, half_turned, half_out_ready = (
            sem(s) for s in ("half_done", "half_joined", "half_turned", "half_out_ready"))

        def wait(eng, semaphore, count):
            if not isinstance(count, int) or count > 0:
                eng.wait_ge(semaphore, count)

        def after(k, q):
            return (k, 1) if q == 0 else (k + 1, 0)

        def before(k, q):
            return (k, 0) if q == 1 else (k - 1, 1)

        PAIRS = B // 2
        HALF = N // 2
        turned_ps = (misc_ps, bwd_ps)

        def later_batches(eng, step):
            step(0, 1, 2)
            with eng.Fori(1, PAIRS - 1) as k:
                step(k, 0, 2)
                step(k, 1, 2)
            step(PAIRS - 1, 0, 1)
            step(PAIRS - 1, 1, 0)

        block = ctx.enter_context(nc.Block())

        @block.sync
        def _(sp):
            def load_x(k, q):
                sp.dma_start(x_sb[q][:], x[2 * k + q, :, :].rearrange("(j p) f -> p j f", p=P)).then_inc(x_loaded[q], 16)

            def load_a(k, q, j):
                sp.dma_start(a_sb[q][:, j, :], adj[2 * k + q, j * P:(j + 1) * P, :]).then_inc(a_loaded[q][j], 16)

            def reload(k, q):
                b = 2 * k + q
                sp.wait_ge(h_ready, b + 1)
                sp.wait_ge(xb_ready, b + 1)
                load_x(k + 1, q)
                sp.wait_ge(a_turned[C - 1], b + 1)
                for j in range(C):
                    sp.wait_ge(a_lo_ready[j], b + 1)
                    load_a(k + 1, q, j)

            def store(k, q):
                sp.wait_ge(out_ready, 2 * k + q + 1)
                sp.dma_start(out[2 * k + q, :, :].rearrange("(j p) o -> p j o", p=P), o_sb[q][:]).then_inc(out_stored[q], 16)

            load_x(0, 0)
            for j in range(C):
                load_a(0, 0, j)
            load_x(0, 1)
            sp.dma_start(we_sb[:], W[:, F:FE, :]).then_inc(we_loaded, 16)
            with nc.allow_non_contiguous_dma(reason="a few hundred bytes, once"):
                sp.dma_start(wedge[:], W_edges.rearrange("r (d one) -> (r d) one", one=1)).then_inc(wedge_loaded, 16)
            for j in range(C):
                load_a(0, 1, j)
            sp.dma_start(w_sb[:], W[:, 0:F, :].rearrange("r f o -> f r o")).then_inc(w_loaded, 16)
            sp.dma_start(bias_sb[:], bias.rearrange("(j p) o -> p j o", p=P)).then_inc(bias_loaded, 16)
            reload(0, 0)
            reload(0, 1)
            with sp.Fori(0, PAIRS - 2) as k:
                store(k, 0)
                reload(k + 1, 0)
                store(k, 1)
                reload(k + 1, 1)
            store(PAIRS - 2, 0)
            store(PAIRS - 2, 1)
            store(PAIRS - 1, 0)
            for half, (ready, count) in enumerate(((half_out_ready, 1), (out_ready, B))):
                sp.wait_ge(ready, count)
                sp.dma_start(out[B - 1, half * HALF:(half + 1) * HALF, :].rearrange("(j p) o -> p j o", p=P),
                             o_sb[1][:, half * C // 2:(half + 1) * C // 2, :]).then_inc(out_stored[1], 16)
            sp.wait_ge(out_stored[0], 16 * PAIRS)
            sp.wait_ge(out_stored[1], 16 * (PAIRS + 1))

        @block.gpsimd
        def _(pool):
            def reciprocal_std(k, q):
                b = 2 * k + q
                pool.wait_ge(mean_var_ready, b + 1)
                wait(pool, h_ready, b - 1)
                pool.tensor_tensor(var_eps[q][:], mean_var[q][:, :, 1], eps[:], ALU.add)
                pool.tensor_tensor(neg_mean[q][:], mean_var[q][:, :, 0], minus_one[:], ALU.mult).then_inc(ve_ready, 1)
                pool.wait_ge(ve_ready, b + 1)
                pool.tensor_tensor(rstd[q][:], var_eps[q][:], minus_half[:], ALU.pow).then_inc(rstd_ready, 1)
                pool.wait_ge(rstd_ready, b + 1)
                pool.tensor_tensor(shift[q][:], neg_mean[q][:], rstd[q][:], ALU.mult).then_inc(shift_ready, 1)

            def split_a(k, q, j):
                b = 2 * k + q
                pool.wait_ge(a_hi_ready[j], b + 1)
                wait(pool, bwd_done, b - 1)
                pool.tensor_tensor(a_lo[q][:, j, :], a_sb[q][:, j, :], a_hi[q][:, j, :].bitcast(fp32),
                                   ALU.subtract).then_inc(a_lo_ready[j], 1)

            def split_h(k, q):
                b = 2 * k + q
                pool.wait_ge(h_hi_ready, b + 1)
                wait(pool, fwd_done, b - 1)
                pool.tensor_tensor(h_lo[q][:], h_sb[q][:], h_hi[q][:].bitcast(fp32),
                                   ALU.subtract).then_inc(h_lo_ready, 1)

            def add_bias(k, q):
                b = 2 * k + q
                pool.wait_ge(x_loaded[q], 16 * (k + 1))
                wait(pool, out_ready, b - 1)
                pool.tensor_tensor(xb_sb[q][:], x_sb[q][:], bias_sb[:], ALU.add).then_inc(xb_ready, 1)

            def parts_of(q, t, part):
                quarters = sum_parts[q][:, 2 * t:2 * t + 2, 0:K4 * C]
                return quarters.rearrange("p g (j k) -> p g j k", k=K4)[:, :, :, part::2]

            def sums_of(q, t):
                return sums[q][:, t, :].unsqueeze(1).unsqueeze(3).to_broadcast([P, 2, C, 2])

            def split_sums(k, q):
                b = 2 * k + q
                wait(pool, sums_turned, b - 1)
                pool.wait_ge(a_hi_ready[C - 1], b + 1)
                pool.wait_ge(at_hi_ready[C - 1], b + 1)
                for t in range(2):
                    last = pool.tensor_tensor(parts_of(q, t, 0), sums_of(q, t), ones[:], ALU.mult)
                last.then_inc(sum_hi_ready, 1)
                pool.wait_ge(sum_hi_ready, b + 1)
                for t in range(2):
                    last = pool.tensor_tensor(parts_of(q, t, 1), sums_of(q, t), parts_of(q, t, 0).bitcast(fp32),
                                              ALU.subtract)
                last.then_inc(sums_split, 1)

            def first_step():
                ahead = (0, 1)
                pool.wait_ge(parts_zeroed, 1)
                split_sums(0, 0)
                pool.wait_ge(w_hi_ready, 1)
                pool.tensor_tensor(w_lo[:, W_DVE:, :], w_sb[:, W_DVE:, :], w_hi[:, W_DVE:, :].bitcast(fp32),
                                   ALU.subtract).then_inc(w_lo_ready, 1)
                pool.wait_ge(bias_loaded, 16)
                add_bias(0, 0)
                reciprocal_std(*ahead)
                split_a(*ahead, 0)
                split_a(*ahead, 1)
                split_h(*ahead)
                split_a(*ahead, 2)
                split_a(*ahead, 3)
                add_bias(*ahead)

            def step(k, q, left):
                split_sums(k, q)
                if left:
                    ahead = after(k, q)
                    reciprocal_std(*ahead)
                    split_a(*ahead, 0)
                    split_a(*ahead, 1)
                    split_a(*ahead, 2)
                    split_h(*ahead)
                    split_a(*ahead, 3)
                    add_bias(*ahead)

            pool.memset(ident[:], 0.0).then_inc(ident_zeroed, 1)
            pool.memset(minus_half[:], -0.5)
            pool.memset(eps[:], EPS)
            pool.memset(minus_one[:], -1.0)
            pool.memset(ones[:], 1.0).then_inc(consts_ready, 1)
            pool.wait_ge(ident_zeroed, 1)
            pool.affine_select(out=ident[:], in_=ident[:], compare_op=ALU.not_equal, fill=1.0, base=0,
                               pattern=[[-1, P]], channel_multiplier=1).then_inc(ident_ready, 1)
            pool.wait_ge(consts_ready, 1)
            for q in range(2):
                last = pool.memset(sum_parts[q][:].bitcast(fp32), 0.0)
            last.then_inc(parts_zeroed, 1)
            pool.wait_ge(ve_ready, 1)
            pool.tensor_tensor(rstd[0][:], var_eps[0][:], minus_half[:], ALU.pow).then_inc(rstd_ready, 1)
            for j in range(1, C):
                chunk, last = h_sb[0][:, j, :], j == C - 1
                pool.wait_ge(h_hi_ready if last else h0_hi_ready, 1 if last else j + 1)
                pool.tensor_tensor(h_lo[0][:, j, :], chunk, h_hi[0][:, j, :].bitcast(fp32),
                                   ALU.subtract).then_inc(h_lo_ready if last else h0_lo_ready, 1)
            first_step()
            later_batches(pool, step)

        @block.scalar
        def _(act):
            def round_a(k, q, j):
                b = 2 * k + q
                act.wait_ge(a_loaded[q][j], 16 * (k + 1))
                wait(act, bwd_done, b - 1)
                wait(act, sums_split, b - 1)
                act.activation(a_hi[q][:, j, :], a_sb[q][:, j, :], ACT.Copy,
                               accum_out=sums[q][:, 0, j:j + 1]).then_inc(a_hi_ready[j], 1)

            def round_at(k, q, i):
                b = 2 * k + q
                act.wait_ge(a_turned[i], b + 1)
                wait(act, fwd_done, b - 1)
                act.activation(at_hi[q][:, i, :], at_bank(b, i)[:], ACT.Copy,
                               accum_out=sums[q][:, 1, i:i + 1]).then_inc(at_hi_ready[i], 1)

            def normalise(k, q):
                b = 2 * k + q
                act.wait_ge(x_loaded[q], 16 * (k + 1))
                act.wait_ge(shift_ready, b + 1)
                wait(act, h_lo_ready, b - 1)
                wait(act, h_turned, b - 1)
                for j in range(C):
                    last = act.activation(h_sb[q][:, j, :], x_sb[q][:, j, :], ACT.Relu,
                                          bias=shift[q][:, j:j + 1], scale=rstd[q][:, j:j + 1])
                last.then_inc(h_ready, 1)

            def round_ht(k, q):
                b = 2 * k + q
                act.wait_ge(h_turned, b + 1)
                wait(act, rel_done[EYE[-1]], b - 1)
                act.activation(ht_hi[q][:], misc_ps[:], ACT.Copy).then_inc(ht_hi_ready, 1)

            def round_fwd(b):
                act.wait_ge(fwd_done, b + 1)
                wait(act, rel_done[FWD[-1]], b)
                act.activation(fwd_hi[:], fwd_ps[:], ACT.Copy).then_inc(fwd_hi_ready, 1)

            def round_bwd(b):
                act.wait_ge(bwd_done, b + 1)
                wait(act, rel_done[BWD[-1]], b)
                act.activation(bwd_hi[:], bwd_ps[:], ACT.Copy).then_inc(bwd_hi_ready, 1)

            def rows_of_sums(b):
                act.wait_ge(sums_turned, b + 1)
                wait(act, rel_done[FWD[-1]], b)
                for j in range(C):
                    last = act.activation(sum_rows[:, j * P:(j + 1) * P], misc_ps[:, 0:P], ACT.Copy,
                                          scale=own_chunk[:, j:j + 1])
                last.then_inc(sum_rows_ready, 1)

            def join_first(b):
                r = ORDER[0]
                act.wait_ge(rel_done[r], b + 1)
                wait(act, best_turned, b)
                act.activation(best[:], rel_ps[BANK[r]][:], ACT.Identity,
                               bias=c_col[:, r:r + 1]).then_inc(joined[r], 1)

            def first_step():
                ahead = (0, 1)
                act.wait_ge(w_loaded, 16)
                act.activation(w_hi[:], w_sb[:], ACT.Copy).then_inc(w_hi_ready, 1)
                round_bwd(0)
                round_a(*ahead, 0)
                round_a(*ahead, 1)
                act.wait_ge(own_chunk_ready, 1)
                rows_of_sums(0)
                act.wait_ge(c_ready, 1)
                join_first(0)
                act.wait_ge(c_turned, 1)
                act.activation(c_rows[:], at_ps[1][:, 0:O], ACT.Copy).then_inc(c_rows_ready, 1)
                round_fwd(0)
                round_at(*ahead, 0)
                normalise(*ahead)
                round_at(*ahead, 1)
                round_a(*ahead, 2)
                round_at(*ahead, 2)
                round_a(*ahead, 3)
                round_at(*ahead, 3)
                round_ht(*ahead)

            def step(k, q, left):
                b = 2 * k + q
                if left:
                    ahead = after(k, q)
                    round_a(*ahead, 0)
                    round_a(*ahead, 1)
                    round_at(*ahead, 0)
                    round_a(*ahead, 2)
                    round_at(*ahead, 1)
                round_bwd(b)
                if left:
                    normalise(*ahead)
                    round_at(*ahead, 2)
                rows_of_sums(b)
                round_fwd(b)
                join_first(b)
                if left:
                    round_a(*ahead, 3)
                    round_at(*ahead, 3)
                    round_ht(*ahead)

            act.wait_ge(ident_ready, 1)
            act.activation(ident_r[:], ident[:], ACT.Copy).then_inc(ident_r_ready, 1)

            def normalise_chunk(j):
                act.activation(h_sb[0][:, j, :], x_sb[0][:, j, :], ACT.Relu, bias=shift[0][:, j:j + 1],
                               scale=rstd[0][:, j:j + 1]).then_inc(h_ready if j == C - 1 else h0_ready, 1)

            for j in range(C - 1):
                round_a(0, 0, j)
            act.wait_ge(x_loaded[0], 16)
            act.wait_ge(shift_ready, 1)
            for j in range(C):
                normalise_chunk(j)
            round_a(0, 0, C - 1)
            for i in range(C):
                round_at(0, 0, i)
            round_ht(0, 0)
            first_step()
            later_batches(act, step)

        @block.vector
        def _(dve):
            def moments(k, q):
                b = 2 * k + q
                dve.wait_ge(x_loaded[q], 16 * (k + 1))
                for j in range(C):
                    last = dve.bn_stats(stats[q][:, j, :], x_sb[q][:, j, :])
                last.then_inc(bn_done, 1)

            def mean_and_variance(k, q):
                for j in range(C):
                    last = dve.bn_aggr(mean_var[q][:, j, :], stats[q][:, j, :])
                last.then_inc(mean_var_ready, 1)

            def round_h(k, q):
                b = 2 * k + q
                dve.wait_ge(h_ready, b + 1)
                wait(dve, fwd_done, b - 1)
                dve.tensor_copy(h_hi[q][:], h_sb[q][:]).then_inc(h_hi_ready, 1)

            def split_at(k, q, i):
                b = 2 * k + q
                dve.wait_ge(at_hi_ready[i], b + 1)
                wait(dve, fwd_done, b - 1)
                dve.tensor_tensor(at_lo[q][:, i, :], at_bank(b, i)[:], at_hi[q][:, i, :].bitcast(fp32),
                                  ALU.subtract).then_inc(at_lo_ready[i], 1)

            def split_ht(k, q):
                b = 2 * k + q
                dve.wait_ge(ht_hi_ready, b + 1)
                wait(dve, rel_done[EYE[-1]], b - 1)
                dve.tensor_tensor(ht_lo[q][:], misc_ps[:], ht_hi[q][:].bitcast(fp32),
                                  ALU.subtract).then_inc(ht_lo_ready, 1)

            def split_fwd(b):
                dve.wait_ge(fwd_hi_ready, b + 1)
                dve.tensor_tensor(fwd_lo[:], fwd_ps[:], fwd_hi[:].bitcast(fp32),
                                  ALU.subtract).then_inc(fwd_lo_ready, 1)

            def split_bwd(b):
                dve.wait_ge(bwd_hi_ready, b + 1)
                dve.tensor_tensor(bwd_lo[:], bwd_ps[:], bwd_hi[:].bitcast(fp32),
                                  ALU.subtract).then_inc(bwd_lo_ready, 1)

            def join(b, s):
                r = ORDER[s]
                dve.wait_ge(rel_done[r], b + 1)
                dve.wait_ge(joined[ORDER[s - 1]], b + 1)
                if r in EYE:
                    dve.scalar_tensor_tensor(out=best[:], in0=rel_ps[BANK[r]][:], scalar=c_col[:, r:r + 1],
                                             in1=best[:], op0=ALU.add, op1=ALU.max).then_inc(joined[r], 1)
                else:
                    dve.tensor_tensor(best[:], rel_ps[BANK[r]][:], best[:], ALU.max).then_inc(joined[r], 1)

            def finish(k, q):
                b = 2 * k + q
                dve.wait_ge(best_turned, b + 1)
                dve.wait_ge(xb_ready, b + 1)
                wait(dve, out_stored[q], 16 * k)
                dve.tensor_tensor(o_sb[q][:].rearrange("p j o -> p (j o)"), misc_ps[:],
                                  xb_sb[q][:].rearrange("p j o -> p (j o)"), ALU.add).then_inc(out_ready, 1)

            def c_part(r, part):
                quarter = c_parts[:, RANK1.index(r), 0:K4 * C].rearrange("p (j k) -> p j k", k=K4)
                return quarter[:, :, 2 * part:2 * part + 2], c_col[:, r:r + 1].unsqueeze(2).to_broadcast([P, C, 2])

            def split_c():
                dve.wait_ge(c_ready, 1)
                dve.wait_ge(c_zeroed, 1)
                for r in RANK1:
                    hi, c = c_part(r, 0)
                    last = dve.tensor_copy(hi, c)
                last.then_inc(c_hi_ready, 1)
                dve.wait_ge(c_hi_ready, 1)
                for r in RANK1:
                    (hi, c), (lo, _) = c_part(r, 0), c_part(r, 1)
                    last = dve.tensor_tensor(lo, c, hi.bitcast(fp32), ALU.subtract)
                last.then_inc(c_split, 1)

            def first_step():
                ahead = (0, 1)
                dve.wait_ge(w_hi_ready, 1)
                dve.tensor_tensor(w_lo[:, :W_DVE, :], w_sb[:, :W_DVE, :], w_hi[:, :W_DVE, :].bitcast(fp32),
                                  ALU.subtract).then_inc(w_lo_ready, 1)
                moments(0, 1)
                dve.wait_ge(bn_done, 2)
                mean_and_variance(0, 1)
                split_c()
                split_bwd(0)
                join(0, 1)
                split_fwd(0)
                join(0, 2)
                join(0, 3)
                round_h(*ahead)
                split_at(*ahead, 0)
                split_at(*ahead, 1)
                join(0, 4)
                join(0, 5)
                split_at(*ahead, 2)
                join(0, 6)
                split_at(*ahead, 3)
                split_ht(*ahead)
                moments(1, 0)
                dve.wait_ge(bn_done, 3)
                mean_and_variance(1, 0)

            def step(k, q, left):
                b = 2 * k + q
                if left:
                    ahead = after(k, q)
                    split_at(*ahead, 0)
                    split_at(*ahead, 1)
                finish(*before(k, q))
                split_bwd(b)
                if left:
                    round_h(*ahead)
                    split_at(*ahead, 2)
                if left > 1:
                    moments(k + 1, q)
                    dve.wait_ge(bn_done, b + 3)
                join(b, 1)
                split_fwd(b)
                join(b, 2)
                join(b, 3)
                if left:
                    split_at(*ahead, 3)
                if left > 1:
                    mean_and_variance(k + 1, q)
                join(b, 4)
                if left:
                    split_ht(*ahead)
                join(b, 5)
                if left:
                    join(b, 6)

            dve.memset(warm[:].bitcast(fp32), 0.0).then_inc(warm_zeroed, 1)
            dve.memset(c_parts[:].bitcast(fp32), 0.0).then_inc(c_zeroed, 1)
            dve.wait_ge(ident_ready, 1)
            dve.tensor_reduce(own_relation[:], ident[0:R * REL, 0:R * REL].rearrange("p (r d) -> p r d", d=REL),
                              mybir.AxisListType.X, ALU.add).then_inc(own_relation_ready, 1)
            dve.tensor_reduce(own_chunk[:], ident[:].rearrange("p (g j k) -> p j g k", g=G, k=K4),
                              mybir.AxisListType.XY, ALU.add).then_inc(own_chunk_ready, 1)
            moments(0, 0)
            dve.wait_ge(bn_done, 1)
            mean_and_variance(0, 0)
            dve.wait_ge(mean_var_ready, 1)
            dve.wait_ge(consts_ready, 1)
            dve.tensor_tensor(var_eps[0][:], mean_var[0][:, :, 1], eps[:], ALU.add).then_inc(ve_ready, 1)

            def split_a(j):
                dve.wait_ge(a_hi_ready[j], 1)
                dve.tensor_tensor(a_lo[0][:, j, :], a_sb[0][:, j, :], a_hi[0][:, j, :].bitcast(fp32),
                                  ALU.subtract).then_inc(a_lo_ready[j], 1)

            def round_h_chunk(j):
                last = j == C - 1
                dve.wait_ge(h_ready if last else h0_ready, 1 if last else j + 1)
                dve.tensor_copy(h_hi[0][:, j, :], h_sb[0][:, j, :]).then_inc(h_hi_ready if last else h0_hi_ready, 1)

            split_a(0)
            split_a(1)
            dve.wait_ge(rstd_ready, 1)
            dve.scalar_tensor_tensor(out=shift[0][:], in0=mean_var[0][:, :, 0], scalar=-1.0, in1=rstd[0][:],
                                     op0=ALU.mult, op1=ALU.mult).then_inc(shift_ready, 1)
            round_h_chunk(0)
            dve.wait_ge(h0_hi_ready, 1)
            dve.tensor_tensor(h_lo[0][:, 0, :], h_sb[0][:, 0, :], h_hi[0][:, 0, :].bitcast(fp32),
                              ALU.subtract).then_inc(h0_lo_ready, 1)
            round_h_chunk(1)
            split_a(2)
            round_h_chunk(2)
            round_h_chunk(3)
            dve.wait_ge(own_relation_ready, 1)
            dve.wait_ge(wedge_loaded, 16)
            dve.tensor_tensor(wedge_cols[:], wedge[:].to_broadcast([R * REL, R]), own_relation[:],
                              ALU.mult).then_inc(wedge_cols_ready, 1)
            split_a(3)
            split_at(0, 0, 0)
            split_at(0, 0, 1)
            dve.wait_ge(c_multiplied, 1)
            dve.tensor_copy(c_col[:], at_ps[0][:, 0:R]).then_inc(c_ready, 1)
            split_at(0, 0, 2)
            split_at(0, 0, 3)
            split_ht(0, 0)
            first_step()
            later_batches(dve, step)
            dve.wait_ge(joined[ORDER[-2]], B)
            for half, (done, count, after_it) in enumerate(((half_done, 1, half_joined),
                                                            (rel_done[ORDER[-1]], B, joined[ORDER[-1]]))):
                cols = slice(half * HALF, (half + 1) * HALF)
                dve.wait_ge(done, count)
                dve.tensor_tensor(best[:, cols], at_ps[half][:, cols], best[:, cols],
                                  ALU.max).then_inc(after_it, 1)
            dve.wait_ge(xb_ready, B)
            dve.wait_ge(out_stored[1], 16 * (PAIRS - 1))
            for half, (turned, count, after_it) in enumerate(((half_turned, 1, half_out_ready),
                                                              (best_turned, B, out_ready))):
                cols = slice(half * HALF, (half + 1) * HALF)
                dve.wait_ge(turned, count)
                dve.tensor_tensor(o_sb[1][:].rearrange("p j o -> p (j o)")[:, cols], turned_ps[half][:, cols],
                                  xb_sb[1][:].rearrange("p j o -> p (j o)")[:, cols], ALU.add).then_inc(after_it, 1)

        @block.tensor
        def _(pe):
            def turn_a(k, q, i):
                b = 2 * k + q
                if i == 0:
                    for j in range(C):
                        pe.wait_ge(a_loaded[q][j], 16 * (k + 1))
                if i >= 2:
                    pe.wait_ge(at_lo_ready[i - 2], b + 1)
                elif i == 1 or not (isinstance(b, int) and b == 1):
                    pe.wait_ge(at_lo_ready[i + 2], b)
                for j in range(C):
                    last = pe.transpose(at_bank(b, i)[:, j * P:(j + 1) * P], a_sb[q][:, j, i * P:(i + 1) * P], ident[:])
                last.then_inc(a_turned[i], 1)

            def turn_h(k, q):
                b = 2 * k + q
                pe.wait_ge(h_ready, b + 1)
                wait(pe, sum_rows_ready, b)
                for j in range(C):
                    last = pe.transpose(misc_ps[:, j * P:(j + 1) * P], h_sb[q][:, j, :], ident[:])
                last.then_inc(h_turned, 1)

            def turn_sums(k, q):
                b = 2 * k + q
                pe.wait_ge(sums_split, b + 1)
                if isinstance(b, int) and b == 0:
                    pe.wait_ge(ht_lo_ready, 1)
                else:
                    pe.wait_ge(out_ready, b)
                pe.matmul(misc_ps[:, 0:P], sum_parts[q][:].rearrange("p g k -> p (g k)"), ident_r[:],
                          start=True, stop=True).then_inc(sums_turned, 1)

            def turn_best(k, q):
                b = 2 * k + q
                pe.wait_ge(joined[ORDER[-1]], b + 1)
                pe.wait_ge(ht_lo_ready, b + 2)
                for j in range(C):
                    last = pe.transpose(misc_ps[:, j * P:(j + 1) * P], best[:, j * P:(j + 1) * P], ident[:])
                last.then_inc(best_turned, 1)

            def passes(out, w_hi_, w_lo_, m_hi, m_lo, start, stop):
                pe.matmul(out, w_hi_, m_hi, start=start, stop=False)
                pe.matmul(out, w_hi_, m_lo, start=False, stop=False)
                return pe.matmul(out, w_lo_, m_hi, start=False, stop=stop)

            def bwd(k, q, j):
                b = 2 * k + q
                if isinstance(b, int) and b == 0 and j < C - 1:
                    pe.wait_ge(h0_hi_ready, j + 1)
                    pe.wait_ge(h0_lo_ready, j + 1)
                elif j == 0 or (isinstance(b, int) and b == 0):
                    pe.wait_ge(h_hi_ready, b + 1)
                    pe.wait_ge(h_lo_ready, b + 1)
                if j == 0:
                    wait(pe, bwd_lo_ready, b)
                pe.wait_ge(a_hi_ready[j], b + 1)
                pe.wait_ge(a_lo_ready[j], b + 1)
                last = passes(bwd_ps[:], h_hi[q][:, j, :], h_lo[q][:, j, :], a_hi[q][:, j, :], a_lo[q][:, j, :],
                              j == 0, j == C - 1)
                if j == C - 1:
                    last.then_inc(bwd_done, 1)

            def fwd(k, q, i):
                b = 2 * k + q
                if i == 0:
                    wait(pe, fwd_lo_ready, b)
                pe.wait_ge(at_hi_ready[i], b + 1)
                pe.wait_ge(at_lo_ready[i], b + 1)
                last = passes(fwd_ps[:], h_hi[q][:, i, :], h_lo[q][:, i, :], at_hi[q][:, i, :], at_lo[q][:, i, :],
                              i == 0, i == C - 1)
                if i == C - 1:
                    last.then_inc(fwd_done, 1)

            def relation(k, q, r):
                b = 2 * k + q
                if r not in (BWD[1], FWD[1]):
                    prior, back = BEFORE[r]
                    wait(pe, joined[prior], b + 1 - back)
                if r == EYE[0]:
                    pe.wait_ge(ht_hi_ready, b + 1)
                    pe.wait_ge(ht_lo_ready, b + 1)
                elif r == BWD[0]:
                    pe.wait_ge(bwd_hi_ready, b + 1)
                    pe.wait_ge(bwd_lo_ready, b + 1)
                elif r == FWD[0]:
                    pe.wait_ge(fwd_hi_ready, b + 1)
                    pe.wait_ge(fwd_lo_ready, b + 1)
                m_hi, m_lo = ((ht_hi[q], ht_lo[q]) if r in EYE else (bwd_hi, bwd_lo) if r in BWD else (fwd_hi, fwd_lo))
                first_of_pair, second_of_pair = r in (BWD[0], FWD[0]), r in (BWD[1], FWD[1])
                last = passes(rel_ps[BANK[r]][:], w_hi[:, r, :], w_lo[:, r, :], m_hi[:], m_lo[:],
                              not second_of_pair, not first_of_pair)
                if not first_of_pair:
                    last.then_inc(rel_done[r], 1)

            def rank_one(r, start, to=None, cols=slice(0, N)):
                to = rel_ps[BANK[r]] if to is None else to
                rows = slice(QUARTER * RANK1.index(r), QUARTER * (RANK1.index(r) + 1))
                return pe.matmul(to[:, cols], c_rows[rows, :], sum_rows[rows, cols],
                                 start=start, stop=not start)

            def rank_ones(k, q, r0, r1):
                b = 2 * k + q
                prior, back = BEFORE[r1]
                pe.wait_ge(joined[prior], b + 1 - back)
                if r0 == BWD[0]:
                    pe.wait_ge(sum_rows_ready, b + 1)
                rank_one(r0, False).then_inc(rel_done[r0], 1)
                rank_one(r1, True)

            def first_step():
                ahead = (0, 1)
                for j in range(C):
                    bwd(0, 0, j)
                turn_h(0, 0)
                pe.wait_ge(we_loaded, 16)
                pe.wait_ge(wedge_cols_ready, 1)
                pe.matmul(at_ps[0][:, 0:R], we_sb[:], wedge_cols[:], start=True, stop=True).then_inc(c_multiplied, 1)
                fwd(0, 0, 0)
                fwd(0, 0, 1)
                pe.wait_ge(c_ready, 1)
                turn_a(*ahead, 0)
                fwd(0, 0, 2)
                fwd(0, 0, 3)
                turn_sums(0, 0)
                pe.wait_ge(w_hi_ready, 1)
                pe.wait_ge(w_lo_ready, 2)
                relation(0, 0, EYE[0])
                relation(0, 0, EYE[1])
                relation(0, 0, EYE[2])
                pe.wait_ge(c_split, 1)
                pe.wait_ge(ident_r_ready, 1)
                pe.wait_ge(at_lo_ready[C - 1], 1)
                pe.matmul(at_ps[1][:, 0:O], c_parts[:].rearrange("p g k -> p (g k)"), ident_r[:],
                          start=True, stop=True).then_inc(c_turned, 1)
                relation(0, 0, BWD[0])
                pe.wait_ge(c_rows_ready, 1)
                rank_ones(0, 0, *BWD)
                turn_a(*ahead, 1)
                relation(0, 0, BWD[1])
                relation(0, 0, FWD[0])
                rank_ones(0, 0, *FWD)
                relation(0, 0, FWD[1])
                turn_a(*ahead, 2)
                turn_a(*ahead, 3)
                turn_h(*ahead)

            def step(k, q, left):
                ahead = after(k, q)
                bwd(k, q, 0)
                if left:
                    turn_a(*ahead, 0)
                bwd(k, q, 1)
                bwd(k, q, 2)
                if left:
                    turn_a(*ahead, 1)
                bwd(k, q, 3)
                turn_best(*before(k, q))
                fwd(k, q, 0)
                fwd(k, q, 1)
                if left:
                    turn_a(*ahead, 2)
                turn_sums(k, q)
                fwd(k, q, 2)
                fwd(k, q, 3)
                relation(k, q, EYE[0])
                if left:
                    turn_a(*ahead, 3)
                relation(k, q, EYE[1])
                relation(k, q, EYE[2])
                relation(k, q, BWD[0])
                rank_ones(k, q, *BWD)
                relation(k, q, BWD[1])
                if left:
                    turn_h(*ahead)
                relation(k, q, FWD[0])
                if left:
                    rank_ones(k, q, *FWD)
                    relation(k, q, FWD[1])

            pe.wait_ge(warm_zeroed, 1)
            for _ in range(WARM):
                pe.matmul(bwd_ps[:], warm[:, 0:P], warm[:], start=True, stop=True)
            pe.wait_ge(ident_ready, 1)
            for j in range(C):
                pe.wait_ge(a_loaded[0][j], 16)
                for i in range(C):
                    last = pe.transpose(at_bank(0, i)[:, j * P:(j + 1) * P], a_sb[0][:, j, i * P:(i + 1) * P], ident[:])
                    if j == C - 1:
                        last.then_inc(a_turned[i], 1)
            first_step()
            later_batches(pe, step)
            rank_one(FWD[0], False).then_inc(rel_done[FWD[0]], 1)
            r = ORDER[-1]
            for half, done in enumerate((half_done, rel_done[r])):
                cols = slice(half * HALF, (half + 1) * HALF)
                passes(at_ps[half][:, cols], w_hi[:, r, :], w_lo[:, r, :], fwd_hi[:, cols], fwd_lo[:, cols],
                       True, False)
                rank_one(r, False, at_ps[half], cols).then_inc(done, 1)
            pe.wait_ge(sum_rows_ready, B)
            for half, (ready, count, after_it) in enumerate(((half_joined, 1, half_turned),
                                                             (joined[r], B, best_turned))):
                pe.wait_ge(ready, count)
                for j in range(half * C // 2, (half + 1) * C // 2):
                    last = pe.transpose(turned_ps[half][:, j * P:(j + 1) * P], best[:, j * P:(j + 1) * P], ident[:])
                last.then_inc(after_it, 1)


_INS = ["x", "adj", "L0_gnn_W", "L0_gnn_W_edges", "L0_gnn_b"]


def kernel(**inputs):
    import numpy as np
    import concourse.bacc as bacc
    from concourse import mybir
    from concourse.bass_utils import run_bass_kernel_spmd

    nc = bacc.Bacc("TRN2", target_bir_lowering=False, num_devices=1)
    arrays, args = {}, []
    for name in _INS:
        a = np.ascontiguousarray(inputs[name])
        arrays[f"in_{name}"] = a
        args.append(nc.dram_tensor(f"in_{name}", a.shape, mybir.dt.from_np(a.dtype), kind="ExternalInput").ap())
    out = nc.dram_tensor("out", inputs["x"].shape, mybir.dt.float32, kind="ExternalOutput").ap()
    gnn_layer(nc, *args, out)
    r = run_bass_kernel_spmd(nc, [arrays], core_ids=[0])
    return r.results[0]["out"]
```
